# Optimizing a Trainium2 kernel written in Bass

```python
import numpy as np
import jax
import jax.numpy as jnp

def _softmax(x, axis=-1):
    return jax.nn.softmax(x, axis=axis)

def _gelu(x):
    return jax.nn.gelu(x, approximate=True)

def _silu(x):
    return jax.nn.silu(x)

def _sigmoid(x):
    return jax.nn.sigmoid(x)

def _layernorm(x, axis=-1, eps=1e-05):
    m = jnp.mean(x, axis=axis, keepdims=True)
    v = jnp.var(x, axis=axis, keepdims=True)
    return (x - m) / jnp.sqrt(v + eps)

def _scatter_add(tgt, idx, src, axis=0):
    return tgt.at[idx].add(src)

def _segment_sum(src, seg, n):
    return jax.ops.segment_sum(src, seg, n)
kernel_name = 'mk_gnn_preln_d4_gnn_r32_772ee2'

def setup_inputs(seed: int=0):
    np.random.seed(seed)
    _w = jnp.asarray

    def _rec_inputs():
        import jax
        import jax.numpy as jnp
        _gk = jax.random.key(seed)
        x = -0.0001006 + 1 * jax.random.normal(jax.random.fold_in(_gk, 1), (3125, 96), jnp.float32)
        _s = jax.random.randint(jax.random.fold_in(_gk, 2), (25000,), 0, 3125, jnp.int32)
        _d = jax.random.randint(jax.random.fold_in(_gk, 3), (25000,), 0, 3125, jnp.int32)
        _loop = jnp.arange(3125, dtype=jnp.int32)
        src = jnp.concatenate([_s, _d, _loop])
        dst = jnp.concatenate([_d, _s, _loop])
        _o = jnp.argsort(dst, stable=True)
        src = src[_o]
        dst = dst[_o]
        edge_attr_4 = 0.000714719 + 1.00021 * jax.random.normal(jax.random.fold_in(_gk, 11), (53125, 4), jnp.float32)
        return (x, src, dst, edge_attr_4)
    x, src, dst, edge_attr_4 = _rec_inputs()

    def _L0_gnn_setup():
        import jax, jax.numpy as jnp
        import numpy as np
        N_NODES = 50000
        N_EDGES = 25000
        D = 96
        N_LAYERS = 3
        key = jax.random.key(seed)
        ks = jax.random.split(key, 8)
        s = 1.0 / np.sqrt(D)
        x = jax.random.normal(ks[0], (N_NODES, D), dtype=jnp.float32)
        edge_index = jax.random.randint(ks[1], (2, N_EDGES), 0, N_NODES, dtype=jnp.int32)
        W_in = jax.random.normal(ks[2], (D, D), dtype=jnp.float32) * s
        b_in = jnp.zeros((D,), dtype=jnp.float32)
        gcn_W = jax.random.normal(ks[3], (N_LAYERS, D, D), dtype=jnp.float32) * s
        gcn_b = jnp.zeros((N_LAYERS, D), dtype=jnp.float32)
        W_out = jax.random.normal(ks[4], (D, D), dtype=jnp.float32) * s
        b_out = jnp.zeros((D,), dtype=jnp.float32)
        return {'x': x, 'edge_index': edge_index, 'W_in': W_in, 'b_in': b_in, 'gcn_W': gcn_W, 'gcn_b': gcn_b, 'W_out': W_out, 'b_out': b_out}
    _L0_gnn_all = _L0_gnn_setup()
    _L0_gnn_in = {k: v for k, v in _L0_gnn_all.items() if k in ('W_in', 'b_in', 'gcn_W', 'gcn_b', 'W_out', 'b_out')}
    del _L0_gnn_all

    def _L1_gnn_setup():
        import jax, jax.numpy as jnp
        import numpy as np
        EPS = 1e-05

        def _mlp(h, W, b, gamma, beta):
            h = jax.nn.relu(h @ W + b)
            mu = jnp.mean(h, axis=0)
            var = jnp.mean(jnp.square(h - mu), axis=0)
            return gamma * (h - mu) * jax.lax.rsqrt(var + EPS) + beta
        key = jax.random.key(seed)
        ks = jax.random.split(key, 10)
        N, E, C_in, C_out, E_dim = (50000, 25000, 96, 96, 4)
        x = jax.random.normal(ks[0], (N, C_in), dtype=jnp.float32)
        edge_index = jax.random.randint(ks[1], (2, E), 0, N, dtype=jnp.int64)
        edge_attr = jax.random.normal(ks[2], (E, E_dim), dtype=jnp.float32)
        s = lambda fan_in: 1.0 / np.sqrt(fan_in)
        W_node = jax.random.uniform(ks[3], (C_in, C_out), jnp.float32, -s(C_in), s(C_in))
        b_node = jnp.zeros((C_out,), jnp.float32)
        g_node = jnp.ones((C_out,), jnp.float32)
        beta_node = jnp.zeros((C_out,), jnp.float32)
        W_edge = jax.random.uniform(ks[4], (E_dim, C_out), jnp.float32, -s(E_dim), s(E_dim))
        b_edge = jnp.zeros((C_out,), jnp.float32)
        g_edge = jnp.ones((C_out,), jnp.float32)
        beta_edge = jnp.zeros((C_out,), jnp.float32)
        M_in = 2 * C_in + C_out
        W_msg = jax.random.uniform(ks[5], (M_in, C_out), jnp.float32, -s(M_in), s(M_in))
        b_msg = jnp.zeros((C_out,), jnp.float32)
        g_msg = jnp.ones((C_out,), jnp.float32)
        beta_msg = jnp.zeros((C_out,), jnp.float32)
        return dict(x=x, edge_index=edge_index, edge_attr=edge_attr, W_node=W_node, b_node=b_node, g_node=g_node, beta_node=beta_node, W_edge=W_edge, b_edge=b_edge, g_edge=g_edge, beta_edge=beta_edge, W_msg=W_msg, b_msg=b_msg, g_msg=g_msg, beta_msg=beta_msg)
    _L1_gnn_all = _L1_gnn_setup()
    _L1_gnn_in = {k: v for k, v in _L1_gnn_all.items() if k in ('W_node', 'b_node', 'g_node', 'beta_node', 'W_edge', 'b_edge', 'g_edge', 'beta_edge', 'W_msg', 'b_msg', 'g_msg', 'beta_msg')}
    del _L1_gnn_all

    def _L2_gnn_setup():
        import jax, jax.numpy as jnp
        import numpy as np
        N_NODES = 50000
        N_EDGES = 25000
        D_IN = 96
        D_OUT = 96
        NEG_SLOPE = 0.2
        key = jax.random.key(seed)
        k1, k2, k3, k4, k5 = jax.random.split(key, 5)
        x = jax.random.normal(k1, (N_NODES, D_IN), dtype=jnp.float32)
        W = jax.random.normal(k2, (D_IN, D_OUT), dtype=jnp.float32) * (1.0 / np.sqrt(D_IN))
        att_src = jax.random.normal(k3, (D_OUT,), dtype=jnp.float32) * 0.1
        att_dst = jax.random.normal(k4, (D_OUT,), dtype=jnp.float32) * 0.1
        bias = jnp.zeros((D_OUT,), dtype=jnp.float32)
        edge_index = jax.random.randint(k5, (2, N_EDGES), 0, N_NODES, dtype=jnp.int64)
        return {'x': x, 'W': W, 'att_src': att_src, 'att_dst': att_dst, 'bias': bias, 'edge_index': edge_index}
    _L2_gnn_all = _L2_gnn_setup()
    _L2_gnn_in = {k: v for k, v in _L2_gnn_all.items() if k in ('W', 'att_src', 'att_dst', 'bias')}
    del _L2_gnn_all

    def _L3_gnn_setup():
        import jax, jax.numpy as jnp
        import numpy as np
        BN_EPS = 1e-05
        key = jax.random.key(seed)
        ks = jax.random.split(key, 5)
        N, E, D = (50000, 25000, 96)
        x = jax.random.normal(ks[0], (N, D), dtype=jnp.float32)
        edge_index = jax.random.randint(ks[1], (2, E), 0, N, dtype=jnp.int64)
        Wl = jax.random.normal(ks[2], (D, D), dtype=jnp.float32) / np.sqrt(D)
        bl = jnp.zeros((D,), dtype=jnp.float32)
        Wr = jax.random.normal(ks[3], (D, D), dtype=jnp.float32) / np.sqrt(D)
        gamma = jnp.ones((D,), dtype=jnp.float32)
        beta = jnp.zeros((D,), dtype=jnp.float32)
        return {'x': x, 'edge_index': edge_index, 'Wl': Wl, 'bl': bl, 'Wr': Wr, 'gamma': gamma, 'beta': beta}
    _L3_gnn_all = _L3_gnn_setup()
    _L3_gnn_in = {k: v for k, v in _L3_gnn_all.items() if k in ('Wl', 'bl', 'Wr', 'gamma', 'beta')}
    del _L3_gnn_all
    return {'x': x, 'src': src, 'dst': dst, 'edge_attr_4': edge_attr_4, 'L0_gnn_W_in': _L0_gnn_in['W_in'], 'L0_gnn_b_in': _L0_gnn_in['b_in'], 'L0_gnn_gcn_W': _L0_gnn_in['gcn_W'], 'L0_gnn_gcn_b': _L0_gnn_in['gcn_b'], 'L0_gnn_W_out': _L0_gnn_in['W_out'], 'L0_gnn_b_out': _L0_gnn_in['b_out'], 'L1_gnn_W_node': _L1_gnn_in['W_node'], 'L1_gnn_b_node': _L1_gnn_in['b_node'], 'L1_gnn_g_node': _L1_gnn_in['g_node'], 'L1_gnn_beta_node': _L1_gnn_in['beta_node'], 'L1_gnn_W_edge': _L1_gnn_in['W_edge'], 'L1_gnn_b_edge': _L1_gnn_in['b_edge'], 'L1_gnn_g_edge': _L1_gnn_in['g_edge'], 'L1_gnn_beta_edge': _L1_gnn_in['beta_edge'], 'L1_gnn_W_msg': _L1_gnn_in['W_msg'], 'L1_gnn_b_msg': _L1_gnn_in['b_msg'], 'L1_gnn_g_msg': _L1_gnn_in['g_msg'], 'L1_gnn_beta_msg': _L1_gnn_in['beta_msg'], 'L2_gnn_W': _L2_gnn_in['W'], 'L2_gnn_att_src': _L2_gnn_in['att_src'], 'L2_gnn_att_dst': _L2_gnn_in['att_dst'], 'L2_gnn_bias': _L2_gnn_in['bias'], 'L3_gnn_Wl': _L3_gnn_in['Wl'], 'L3_gnn_bl': _L3_gnn_in['bl'], 'L3_gnn_Wr': _L3_gnn_in['Wr'], 'L3_gnn_gamma': _L3_gnn_in['gamma'], 'L3_gnn_beta': _L3_gnn_in['beta']}

def reference(x, src, dst, edge_attr_4, L0_gnn_W_in, L0_gnn_b_in, L0_gnn_gcn_W, L0_gnn_gcn_b, L0_gnn_W_out, L0_gnn_b_out, L1_gnn_W_node, L1_gnn_b_node, L1_gnn_g_node, L1_gnn_beta_node, L1_gnn_W_edge, L1_gnn_b_edge, L1_gnn_g_edge, L1_gnn_beta_edge, L1_gnn_W_msg, L1_gnn_b_msg, L1_gnn_g_msg, L1_gnn_beta_msg, L2_gnn_W, L2_gnn_att_src, L2_gnn_att_dst, L2_gnn_bias, L3_gnn_Wl, L3_gnn_bl, L3_gnn_Wr, L3_gnn_gamma, L3_gnn_beta):
    import jax
    import jax.numpy as jnp

    def _L0_gnn_ref(x, edge_index, W_in, b_in, gcn_W, gcn_b, W_out, b_out):
        import jax, jax.numpy as jnp
        import numpy as np
        N_NODES = 50000
        N_EDGES = 25000
        D = 96
        N_LAYERS = 3
        N = x.shape[0]
        loop = jnp.arange(N, dtype=edge_index.dtype)
        row = jnp.concatenate([edge_index[0], loop])
        col = jnp.concatenate([edge_index[1], loop])
        deg = jax.ops.segment_sum(jnp.ones_like(col, dtype=x.dtype), col, num_segments=N)
        dinv = jnp.where(deg > 0, jax.lax.rsqrt(deg), 0.0)
        norm = (dinv[row] * dinv[col])[:, None]

        def gcn_conv(h, W, b):
            hw = h @ W.T
            msg = norm * hw[row]
            out = jax.ops.segment_sum(msg, col, num_segments=N)
            return out + b
        h = jax.nn.relu(x @ W_in.T + b_in)
        for l in range(N_LAYERS):
            h = h + jax.nn.relu(gcn_conv(h, gcn_W[l], gcn_b[l]))
        return h @ W_out.T + b_out

    def _L1_gnn_ref(x, edge_index, edge_attr, W_node, b_node, g_node, beta_node, W_edge, b_edge, g_edge, beta_edge, W_msg, b_msg, g_msg, beta_msg):
        import jax, jax.numpy as jnp
        import numpy as np
        EPS = 1e-05

        def _mlp(h, W, b, gamma, beta):
            h = jax.nn.relu(h @ W + b)
            mu = jnp.mean(h, axis=0)
            var = jnp.mean(jnp.square(h - mu), axis=0)
            return gamma * (h - mu) * jax.lax.rsqrt(var + EPS) + beta
        node_feat = _mlp(x, W_node, b_node, g_node, beta_node)
        edge_feat = _mlp(edge_attr, W_edge, b_edge, g_edge, beta_edge)
        row, col = (edge_index[0], edge_index[1])
        message = jnp.concatenate([x[row], x[col], edge_feat], axis=1)
        message = _mlp(message, W_msg, b_msg, g_msg, beta_msg)
        agg = jax.ops.segment_sum(message, col, num_segments=node_feat.shape[0])
        return agg + node_feat

    def _L2_gnn_ref(x, W, att_src, att_dst, bias, edge_index):
        import jax, jax.numpy as jnp
        import numpy as np
        N_NODES = 50000
        N_EDGES = 25000
        D_IN = 96
        D_OUT = 96
        NEG_SLOPE = 0.2
        N = x.shape[0]
        h = x @ W
        loops = jnp.arange(N, dtype=edge_index.dtype)
        src = jnp.concatenate([edge_index[0], loops])
        dst = jnp.concatenate([edge_index[1], loops])
        a_src = h @ att_src
        a_dst = h @ att_dst
        e = jax.nn.leaky_relu(a_src[src] + a_dst[dst], NEG_SLOPE)
        m = jax.ops.segment_max(e, dst, num_segments=N)
        e = jnp.exp(e - m[dst])
        denom = jax.ops.segment_sum(e, dst, num_segments=N)
        alpha = e / (denom[dst] + 1e-16)
        out = jax.ops.segment_sum(h[src] * alpha[:, None], dst, num_segments=N)
        return jnp.tanh(out + bias)

    def _L3_gnn_ref(x, edge_index, Wl, bl, Wr, gamma, beta):
        import jax, jax.numpy as jnp
        import numpy as np
        BN_EPS = 1e-05
        N = x.shape[0]
        src, dst = (edge_index[0], edge_index[1])
        msg_sum = jax.ops.segment_sum(x[src], dst, num_segments=N)
        deg = jax.ops.segment_sum(jnp.ones_like(src, dtype=x.dtype), dst, num_segments=N)
        neigh_mean = msg_sum / jnp.maximum(deg, 1.0)[:, None]
        h = jnp.einsum('nd,od->no', neigh_mean, Wl) + bl + jnp.einsum('nd,od->no', x, Wr)
        mu = h.mean(axis=0)
        var = h.var(axis=0)
        h = (h - mu) * jax.lax.rsqrt(var + BN_EPS) * gamma + beta
        return jax.nn.relu(h)
    edge_index = jnp.stack([src, dst])
    h = jnp.maximum(_layernorm(x, axis=-1), 0.0)
    x = x + _L0_gnn_ref(h, edge_index, L0_gnn_W_in, L0_gnn_b_in, L0_gnn_gcn_W, L0_gnn_gcn_b, L0_gnn_W_out, L0_gnn_b_out)
    h = jnp.maximum(_layernorm(x, axis=-1), 0.0)
    x = x + _L1_gnn_ref(h, edge_index, edge_attr_4, L1_gnn_W_node, L1_gnn_b_node, L1_gnn_g_node, L1_gnn_beta_node, L1_gnn_W_edge, L1_gnn_b_edge, L1_gnn_g_edge, L1_gnn_beta_edge, L1_gnn_W_msg, L1_gnn_b_msg, L1_gnn_g_msg, L1_gnn_beta_msg)
    h = jnp.maximum(_layernorm(x, axis=-1), 0.0)
    x = x + _L2_gnn_ref(h, L2_gnn_W, L2_gnn_att_src, L2_gnn_att_dst, L2_gnn_bias, edge_index)
    h = jnp.maximum(_layernorm(x, axis=-1), 0.0)
    x = x + _L3_gnn_ref(h, edge_index, L3_gnn_Wl, L3_gnn_bl, L3_gnn_Wr, L3_gnn_gamma, L3_gnn_beta)
    return x

_drawn_inputs = setup_inputs


def setup_inputs(seed=0):
    import zlib

    import numpy as np

    out = dict(_drawn_inputs(seed))
    spreads = {'L0_gnn_b_in': (0.0, 0.1),
     'L0_gnn_gcn_b': (0.0, 0.1),
     'L0_gnn_b_out': (0.0, 0.1),
     'L1_gnn_b_node': (0.0, 0.1),
     'L1_gnn_g_node': (1.0, 0.6),
     'L1_gnn_beta_node': (0.0, 0.665),
     'L1_gnn_b_edge': (0.0, 0.1),
     'L1_gnn_g_edge': (1.0, 0.2),
     'L1_gnn_beta_edge': (0.0, 0.1),
     'L1_gnn_b_msg': (0.0, 0.1),
     'L1_gnn_g_msg': (1.0, 0.2),
     'L1_gnn_beta_msg': (0.0, 0.1),
     'L2_gnn_bias': (0.0, 0.733),
     'L3_gnn_bl': (0.0, 0.8),
     'L3_gnn_gamma': (1.0, 0.6),
     'L3_gnn_beta': (0.0, 0.8)}
    factors = {'L2_gnn_att_src': 5.036, 'L2_gnn_att_dst': 8.0}
    for name, (base, spread) in spreads.items():
        noise = np.random.default_rng([zlib.crc32(name.encode()), seed]).standard_normal(out[name].shape)
        drawn = base * np.exp(spread * noise) if base else spread * noise
        out[name] = jnp.asarray(drawn.astype(out[name].dtype))
    for name, factor in factors.items():
        out[name] = (out[name] * factor).astype(out[name].dtype)
    return out
```

```python
import concourse.bass as bass
import numpy as np
from concourse import mybir
from contextlib import ExitStack

DT = mybir.dt
ALU = mybir.AluOpType
ACT = mybir.ActivationFunctionType
AX = mybir.AxisListType

N, E, D, DE = 3125, 53125, 96, 4
P = 125
B = N // P
T = E // P
W = 10
NWIN = -(-N // W)
NPAD = NWIN * W
U = 8
S = -(-(T + NWIN - 1) // U) * U
RING = 4
AHEAD = 3
SPAD = S + AHEAD
RC, RR = 5, T // 5
ROUND = 12582912.0
G = 5
NG = B // G
PB = [(b * 500, min(500, N - b * 500)) for b in range(7)]
DST = PB[-1:] + PB[:-1]
NCH = T // G
LN_EPS = 1e-5
BN_EPS = 1e-5
LOGIT_BOUND = 40.0
NEG_SLOPE, SOFTMAX_EPS = 0.2, 1e-16
EXPONENT = 0x7F800000
LN_SCALE = 4096.0


def build_program(nc, x, dst_tiles, src_tiles, dst_lanes, dst_runs, src_runs, edge_attr_T, weights_T,
                  weights_msg_edge, edge_W, edge_cols, bias_rows, out):
    fp32, fp16, bf16, i32, i16, u32 = DT.float32, DT.float16, DT.bfloat16, DT.int32, DT.int16, DT.uint32
    ctx = ExitStack()
    with ctx:
        def sb(name, shape, dt):
            return ctx.enter_context(nc.sbuf_tensor(name, shape, dt))

        def sem(name):
            return ctx.enter_context(nc.semaphore(name))

        def carver(region):
            at = [0]

            def take(lanes, words):
                piece = region[0:lanes, at[0]:at[0] + words]
                at[0] += words
                assert at[0] <= region.shape[1], at[0]
                return piece
            return take

        P_dram = nc.dram_tensor("src_part", [N, D], fp32).ap()
        Q_dram = nc.dram_tensor("dst_part", [N, D], fp32).ap()
        F_dram = nc.dram_tensor("dst_part_at_first_edge", [E, D], fp32).ap()
        S_dram = nc.dram_tensor("running_sums", [E, D], fp32).ap()
        F_runs = F_dram.rearrange("(p j) c -> p j c", p=P)
        S_runs = S_dram.rearrange("(p j) c -> p j c", p=P)

        CT = sb("counts_T", [P, B, NPAD], fp16)
        CT_words = CT[:, :, :].rearrange("p b n -> p (b n)").bitcast(fp32)
        NWORDS = B * NPAD // 2
        CT_own = [CT[:, :, :].rearrange("p b n -> p (b n)")[:, 0:(B - 1) * (NPAD + P)].rearrange("p (b w) -> p b w", b=B - 1)[:, :, 0:P],
                  CT[:, B - 1:B, (B - 1) * P:B * P]]
        SETUP = 12600
        POOL_ZEROS, DVE_ZEROS = 5600, 4400
        X = sb("X", [P, B, D], fp32)
        AR = sb("arena", [128, 9125], fp32)
        ident = sb("ident", [P, P], fp32)
        identb = sb("identb", [P, P], bf16)
        ones = sb("ones", [P, P], fp32)
        iota_w = sb("iota_w", [P, B * W], i16)
        WT = sb("weights", [D + 1, 8, D], fp32)
        ROWS = sb("node_row_params", [P, 4, D], fp32)
        node_id = sb("node_id", [P, B], fp32)
        upto_pos = sb("edges_upto", [P, 2, B], fp32)
        dinv = sb("dinv", [P, B], fp32)
        lnm = sb("lnm", [P, B], fp32)
        lnv = sb("lnv", [P, B], fp32)
        row_of = sb("row_of", [P, 2, B], i32)
        bn_rows = sb("bn_rows", [P, 2, D], fp32)
        W3 = sb("W3", [D, D], fp32)
        eW = sb("eW", [DE + 1, D], fp32)
        ecols = sb("ecols", [D, 6], fp32)
        tcol = iota_w[0:D, :].bitcast(fp32)[:, 0:D + 1]

        take = carver(CT_words[:, NWORDS - SETUP:NWORDS])
        rows = take(1, 8 * T).rearrange("p (r t) -> p r t", r=8)
        rows_i = take(1, 2 * T).bitcast(i32).rearrange("p (r t) -> p r t", r=2)
        cols = take(RR, 3 * RC).rearrange("p (r c) -> p r c", r=3)
        e_dst = take(RR, RC * P).bitcast(i32)
        e_src = take(RR, RC * P).bitcast(i32)
        f_q, f_r = take(RR, RC * P), take(RR, RC * P)
        sel = take(RR, RC * S // 2).bitcast(fp16).rearrange("p (c s) -> p c s", c=RC)
        sel_a = take(RR, S // 2).bitcast(fp16)
        tq = take(RR, 4 * RC * P // 2 ).bitcast(fp16).rearrange("p (q c i) -> p q c i", q=4, c=RC)
        wrow = take(P, S)
        trow = take(P, S)
        take = carver(AR)
        keyL = take(P, SPAD)
        keyR = take(P, SPAD)
        onehotL = take(P, U * 64).bitcast(bf16).rearrange("p (r k) -> p r k", r=U)[:, :, 0:P]
        dist = take(P, U * 64).bitcast(bf16).rearrange("p (r k) -> p r k", r=U)[:, :, 0:P]
        onehotR = take(P, 4 * B * W // 2).bitcast(fp16).rearrange("p (r k) -> p r k", r=4)
        win_addr = take(1, S).bitcast(i32)
        iota_s = take(P, S // 2).bitcast(i16)
        below_words = take(P, 3126)
        below = below_words.bitcast(bf16).rearrange("p (q n) -> p q n", q=2)
        run_ring = take(P, 2 * T).bitcast(i32).rearrange("p (r t) -> p r t", r=2)
        node_edge, counted = take(P, 2 * B), take(P, 2 * B)
        run_last = take(P, 1).bitcast(i32)
        ones_b = take(P, 1).bitcast(bf16)[:, 0:1]
        zeros = take(P, G * D)
        esum = take(D, 2 * NCH).rearrange("p (q i) -> p q i", q=2)
        take = carver(below_words)
        attr = take(DE + 1, G * P)
        feat = take(D, G * P)
        feat_sq = take(D, G * P)
        iota_n = X[:, :, :].rearrange("p b c -> p (b c)").bitcast(i16)[:, 0:3126]

        take = carver(AR)
        ea = take(DE + 1, 2 * G * P).rearrange("p (s w) -> p s w", s=2)
        RE = take(D, 2 * G * P).rearrange("p (s w) -> p s w", s=2)
        squares = take(P, G * P)
        SO, Dr = (take(P, 2 * G * D).rearrange("p (s k c) -> p s k c", s=2, k=G) for _ in range(2))
        same = take(P, T)
        QB = take(P, 2 * G * D).rearrange("p (s k c) -> p s k c", s=2, k=G)
        take(P, 4 * G)
        Z = take(P, 4 * G * D).rearrange("p (s k c) -> p s k c", s=4, k=G)
        dst_last = take(P, 1).bitcast(i32)
        iota_f = squares[:, 500:500 + P]
        Y2 = squares[:, 0:G * D]
        sq_acc = take(P, G * D)
        src_idx = take(P, 4 * G).bitcast(i32).rearrange("p (s k) -> p s k", s=4)
        turn = take(1, 1)
        msq = same[:, 0:D]
        dst_sb = QB[:, :, :, :].rearrange("p s k c -> p (s k c)")[:, 0:T].bitcast(i32)
        tail_hot = [AR[0:P, w:w + P] for w in [*range(2400, 2400 + 4 * P, P), *range(3605, 3605 + 11 * P, P),
                                               *range(5150, 5150 + 10 * P, P)]]
        TAILS = AR[0:P, 6450:8850].rearrange("p (b c) -> p b c", c=D)
        take = carver(AR)
        HS = take(P, B * (D + 1)).rearrange("p (b c) -> p b c", b=B)
        acc = take(P, 2 * 500).rearrange("p (s n) -> p s n", s=2)
        att = take(P, 5 * 500).rearrange("p (s n) -> p s n", s=5)
        bend = take(P, 2 * 500).rearrange("p (s n) -> p s n", s=2)
        diag = take(P, 2 * 4 * P).rearrange("p (r c n) -> p r c n", r=2, c=4)
        OX = take(P, 4 * D).rearrange("p (c d) -> p c d", c=4)
        a_src_bend, a_src_key = take(P, B), take(P, B)
        ends = take(P, 2)
        span, inv_span = take(P, 1), take(P, 1)
        cmax, cm, dst_bend = (take(P, B) for _ in range(3))
        deg = sb("deg", [P, B], fp32)
        valid = sb("valid", [P, B], fp32)
        a_src, a_dst = valid[:, :], dinv[:, :]
        dst_first = sb("dst_first", [P, 1], i32)

        H = AR[0:P, 0:2400].rearrange("p (b c) -> p b c", c=D)
        SPL = AR[0:P, 2400:4800].bitcast(fp16).rearrange("p (s b c) -> p s b c", s=2, c=D)
        take = carver(AR[:, 4800:6000])
        top_spread = take(P, P)
        maxima = take(P, len(PB))
        top, half_scale, unscale = take(P, 1), take(P, 1), take(P, 1)
        dinv_unscaled = take(P, B)
        Y = AR[0:P, 2400:4800].rearrange("p (b c) -> p b c", c=D)
        TB = AR[0:D + 1, 6000:9125]
        TMP = [AR[0:P, 6000 + n0:6000 + n0 + nn // P * D].rearrange("p (b c) -> p b c", c=D) for n0, nn in PB]

        PS = ctx.enter_context(nc.psum_tensor("PS", [128, 4096], fp32))
        PT = [PS[:, 1024 * k:1024 * k + 640].rearrange("p (k c) -> p k c", c=128) for k in range(2)]
        PO = [PS[:, 2048 + 1024 * k:2048 + 1024 * k + 640].rearrange("p (k c) -> p k c", c=128) for k in range(2)]

        psR = [PS[0:P, 1024 * k:1024 * k + 640].rearrange("p (k c) -> p k c", c=128)[:, :, 0:D] for k in (1, 2)]
        psE = PT[0][0:D, :, 0:P]
        msg_sq = PS[0:P, 3072:3072 + G * D]
        psF = PS[0:D, 2048:2688].rearrange("p (k c) -> p k c", c=128)[:, :, 0:P]

        PSA = PS[0:P, 1024:1536].rearrange("p (c n) -> p c n", c=4)
        att_rows = [[PS[0:P, 512 * (3 + 2 * k + r):512 * (3 + 2 * k + r) + 512] for r in range(2)] for k in range(2)]
        PSO = [PS[0:P, 512 * k:512 * k + 512].rearrange("p (c n) -> p c n", c=4) for k in range(2)]

        att_w = sem("att_w")
        ends_ready, ends_psum = sem("ends_ready"), sem("ends_psum")
        att_added, att_bounded = sem("att_added"), sem("att_bounded")
        max_step, acc_T, diag_ready, row_psum = (
            sem("max_step"), sem("acc_T"), sem("diag_ready"), sem("row_psum"))
        att_cols, bend_done, exp_done, w_done, att_psum = (
            sem("att_cols"), sem("bend_done"), sem("exp_done"), sem("w_done"), sem("att_psum"))
        turns = sem("turns")
        ox_ready, tanh_done = sem("ox_ready"), sem("tanh_done")
        d_zero, zeros_set = sem("d_zero"), sem("zeros_set")
        attr_ones, ld_attr, sq_read, sq_total = sem("attr_ones"), sem("ld_attr"), sem("sq_read"), sem("sq_total")
        ea_ones, stat_pre, feat_free, stat_sums = sem("ea_ones"), sem("stat_pre"), sem("feat_free"), sem("stat_sums")
        edge_shift, edge_const, edge_const_psum, ld_e = sem("edge_shift"), sem("edge_const"), sem("edge_const_psum"), sem("ld_e")
        ld_ea = [sem(f"ld_ea{k}") for k in range(2)]
        ld_idx = [sem(f"ld_idx{k}") for k in range(4)]
        ld_d = [sem(f"ld_d{k}") for k in range(2)]
        st_s = [sem(f"st_s{k}") for k in range(2)]
        rows_here = [sem(f"rows_here{k}") for k in range(4)]
        pq_ready, p_stored, q_stored, q_first, d_scattered = (
            sem("pq_ready"), sem("p_stored"), sem("q_stored"), sem("q_first"), sem("d_scattered"))
        pre_psum, pre_relu, src_in, z_ready, q_step, s_step, y_done, sq_done, sq_summed, rpart_psum = (
            sem("pre_psum"), sem("pre_relu"), sem("src_in"), sem("z_ready"), sem("q_step"), sem("s_step"), sem("y_done"),
            sem("sq_done"), sem("sq_summed"), sem("rpart_psum"))
        last_idx, last_here, tails_hot, lanes_iota = sem("last_idx"), sem("last_here"), sem("tails_hot"), sem("lanes_iota")
        ld_dst, ld_last, node_part_done, layer_done = sem("ld_dst"), sem("ld_last"), sem("node_part_done"), sem("layer_done")

        def reach(eng, s, v):
            if not isinstance(v, int) or v > 0:
                eng.wait_ge(s, v)

        def chunks(eng, body):
            for c in range(5):
                body(0, c)
            with eng.Fori(0, (NCH - 9) // 4) as it:
                for c in range(5, 9):
                    body(it, c)
            for c in range(5, 9):
                body((NCH - 9) // 4, c)

        def ring(it, c, n):
            return c % n, it * (4 // n) + c // n

        def before(it, c, end=NCH):
            return not isinstance(it, int) or 4 * it + c < end

        def src_blocks(eng, body, last=True):
            for i in range(5):
                body(i, i)
            with eng.Fori(0, (B - 5) // 10 - (not last)) as it:
                for j in range(5, 15):
                    body(it * 10 + j, j % 10)
            if not last:
                for i in range(B - 10, B - 1):
                    body(i, i % 10)

        ld_edges, ld_rows, ld_w, ld_x, ld_p = sem("ld_edges"), sem("ld_rows"), sem("ld_w"), sem("ld_x"), sem("ld_p")
        pool_consts, counts_zero = sem("pool_consts"), sem("counts_zero")
        dve_chain = sem("dve_chain")
        step_rows, step_cols, tile_tables, step_tables, step_tables_used = (
            sem("step_rows"), sem("step_cols"), sem("tile_tables"), sem("step_tables"), sem("step_tables_used"))
        runs_below, runs_below_sum, run_rows_known, runs_counted = (
            sem("runs_below"), sem("runs_below_sum"), sem("run_rows_known"), sem("runs_counted"))
        run_rows_here = [sem(f"run_rows_here{k}") for k in range(2)]
        left_dist, left_hot = sem("left_dist"), sem("left_hot")
        onehots, step_counts, counts_added = sem("onehots"), sem("step_counts"), sem("counts_added")
        h_ready, hT_psum, hT_sbuf = sem("h_ready"), sem("hT_psum"), sem("hT_sbuf")
        prod_psum, prod_used = sem("prod_psum"), sem("prod_used")
        top_ready = sem("top_ready")
        split_ready, agg_psum, agg_sbuf = sem("split_ready"), sem("agg_psum"), sem("agg_sbuf")
        var_ready, std_ready = sem("var_ready"), sem("std_ready")
        y_ready, bn_sum = sem("y_ready"), sem("bn_sum")
        tb_ones = sem("tb_ones")
        out_ready, stored = sem("out_ready"), sem("stored")

        block = ctx.enter_context(nc.Block())

        @block.sync
        def _(sp):
            sp.dma_start(rows_i[:, 0, :], dst_lanes[0:1, :]).then_inc(ld_rows, 16)
            sp.dma_start(rows_i[:, 1, :], dst_lanes[P - 1:P, :]).then_inc(ld_rows, 16)
            sp.dma_start(e_dst.rearrange("p (c i) -> p c i", c=RC), dst_tiles.rearrange("(c r) i -> r c i", c=RC)).then_inc(ld_edges, 16)
            sp.dma_start(e_src.rearrange("p (c i) -> p c i", c=RC), src_tiles.rearrange("(c r) i -> r c i", c=RC)).then_inc(ld_edges, 16)
            with nc.allow_non_contiguous_dma(reason="the last dst of each run"):
                sp.dma_start(run_last, dst_runs[:, T - 1:T]).then_inc(ld_edges, 16)
            for k in range(8):
                sp.dma_start(WT[0:D, k, :], weights_T[k]).then_inc(ld_w, 16)
            sp.dma_start(WT[D:D + 1, :, :], bias_rows[0:8].rearrange("(o k) c -> o k c", o=1)).then_inc(ld_w, 16)
            sp.wait_ge(runs_below, 1)
            sp.dma_start(X[:, :, :], x.rearrange("(b p) c -> p b c", p=P)).then_inc(ld_x, 16)
            for k, row in enumerate((11, 12, 13, 4)):
                sp.dma_start(ROWS[:, k, :], bias_rows[row:row + 1, :].to_broadcast([P, D])).then_inc(ld_p, 16)
            for dram, tile in ((edge_W, eW[:, :]), (edge_cols, ecols[:, 0:2]), (weights_msg_edge, W3[:, :])):
                sp.dma_start(tile, dram).then_inc(ld_e, 16)
            sp.wait_ge(attr_ones, 1)

            sp.wait_ge(zeros_set, 1)

            def load_attr(i):
                sp.dma_start(attr[0:DE, :], edge_attr_T[:, bass.ds(i * (G * P), G * P)]).then_inc(ld_attr, 16)
                sp.dma_start(F_runs[:, bass.ds(i * G, G), :], zeros.rearrange("p (k c) -> p k c", k=G)).then_inc(d_zero, 16)
            load_attr(0)
            with sp.Fori(1, NCH) as i:
                sp.wait_ge(stat_pre, i)
                load_attr(i)
            sp.wait_ge(layer_done, 1)
            for k in range(3):
                sp.dma_start(WT[0:D, k, :], weights_T[8 + k]).then_inc(ld_w, 16)
            sp.dma_start(WT[D:D + 1, 0:3, :], bias_rows[8:11].rearrange("(o k) c -> o k c", o=1)).then_inc(ld_w, 16)
            for k in range(4):
                sp.dma_start(ROWS[:, k, :], bias_rows[14 + k:15 + k, :].to_broadcast([P, D])).then_inc(ld_p, 16)
            sp.dma_start(dst_sb, dst_runs).then_inc(ld_dst, 16)
            sp.wait_ge(pq_ready, 1)
            sp.dma_start(Q_dram.rearrange("(b p) c -> p b c", p=P), H).then_inc(q_stored, 16)
            sp.wait_ge(pq_ready, 2)
            sp.dma_start(P_dram.rearrange("(b p) c -> p b c", p=P), Y).then_inc(p_stored, 16)
            def load_idx(it, c):
                slot, used = ring(it, c, 4)
                reach(sp, rows_here[slot], used * (16 * G))
                sp.dma_start(src_idx[:, slot, :], src_runs[:, bass.ds((it * 4 + c) * G, G)]).then_inc(ld_idx[slot], 16)

            sp.wait_ge(pq_ready, 3)
            for c in range(4):
                load_idx(0, c)
            sp.wait_ge(q_stored, 16)
            sp.wait_ge(p_stored, 16)
            sp.wait_ge(d_scattered, 16 * B)
            sp.wait_ge(ea_ones, 1)

            def load_attr_and_dst(it, c):
                slot, i = c % 2, it * 4 + c
                reach(sp, pre_psum, i - 1)
                sp.dma_start(ea[0:DE, slot, :], edge_attr_T[:, bass.ds(i * (G * P), G * P)]).then_inc(ld_ea[slot], 16)
                if isinstance(i, int) and i == 0:
                    sp.wait_ge(node_part_done, 1)
                    with nc.allow_non_contiguous_dma(reason="the last dst of each run"):
                        sp.dma_start(dst_last, dst_runs[:, T - 1:T]).then_inc(ld_last, 16)
                reach(sp, z_ready, i - 1)
                sp.dma_start(Dr[:, slot, :, :], F_runs[:, bass.ds(i * G, G), :]).then_inc(ld_d[slot], 16)

            def store(it, c):
                i = it * 4 + c
                sp.wait_ge(s_step, i * G + G)
                sp.dma_start(S_runs[:, bass.ds(i * G, G), :], SO[:, c % 2, :, :]).then_inc(st_s[c % 2], 16)

            def traffic(it, c):
                if c and before(it, c + 3):
                    load_idx(it, c + 3)
                if before(it, c + 1):
                    load_attr_and_dst(it, c + 1)
                if c >= 2:
                    store(it, c - 2)

            load_attr_and_dst(0, 0)
            chunks(sp, traffic)
            store((NCH - 9) // 4, 7)
            store((NCH - 9) // 4, 8)
            sp.wait_ge(layer_done, 2)
            for k, row in enumerate((18, 19, 20, 9)):
                sp.dma_start(ROWS[:, k, :], bias_rows[row:row + 1, :].to_broadcast([P, D])).then_inc(ld_p, 16)
            sp.wait_ge(layer_done, 3)
            for k in range(2):
                sp.dma_start(ROWS[:, k, :], bias_rows[21 + k:22 + k, :].to_broadcast([P, D])).then_inc(ld_p, 16)
            for g in range(NG):
                sp.wait_ge(out_ready, g + 1)
                sp.dma_start(out.rearrange("(b p) c -> p b c", p=P)[:, G * g:G * g + G, :], X[:, G * g:G * g + G, :]
                             ).then_inc(stored, 16)
            sp.wait_ge(stored, 16 * NG)

        @block.gpsimd
        def _(pool):
            pool.iota(iota_w[:, :], pattern=[[1, B * W]], base=0, channel_multiplier=0).then_inc(pool_consts, 1)
            pool.iota(iota_s, pattern=[[1, S]], base=0, channel_multiplier=0).then_inc(pool_consts, 1)
            pool.iota(iota_n, pattern=[[1, 3126]], base=0, channel_multiplier=0).then_inc(pool_consts, 1)
            pool.iota(node_id[:, :], pattern=[[P, B]], base=0, channel_multiplier=1,
                      allow_small_or_imprecise_dtypes=True).then_inc(pool_consts, 1)
            pool.memset(ident[:, :], 0.0).then_inc(pool_consts, 1)
            pool.memset(ones[:, :], 1.0).then_inc(pool_consts, 1)
            pool.memset(ones_b, 1.0).then_inc(pool_consts, 1)
            pool.wait_ge(pool_consts, 7)
            pool.affine_select(out=ident[:, :], in_=ident[:, :], compare_op=ALU.not_equal, fill=1.0,
                               base=0, pattern=[[-1, P]], channel_multiplier=1).then_inc(pool_consts, 1)
            pool.wait_ge(pool_consts, 8)
            pool.tensor_copy(identb[:, :], ident[:, :]).then_inc(pool_consts, 1)
            pool.memset(CT_words[:, 0:NWORDS - SETUP], 0.0).then_inc(counts_zero, 1)
            pool.memset(zeros, 0.0).then_inc(zeros_set, 1)
            pool.wait_ge(run_rows_known, 1)
            pool.memset(CT_words[:, NWORDS - SETUP:NWORDS - SETUP + POOL_ZEROS], 0.0).then_inc(counts_zero, 1)
            for q in range(2):
                for b in range(B):
                    n = q * B + b
                    if n >= 2:
                        pool.wait_ge(runs_counted, n - 1)
                    pool.indirect_dma_start(out=run_ring[:, n % 2, :], out_offset=None, in_=dst_runs,
                                            in_offset=bass.IndirectOffsetOnAxis(ap=row_of[:, q, b:b + 1].bitcast(u32), axis=0)
                                            ).then_inc(run_rows_here[n % 2], 16)

            pool.wait_ge(pq_ready, 1)
            pool.wait_ge(d_zero, 16 * NCH)
            for b in range(B):
                pool.indirect_dma_start(out=F_dram, out_offset=bass.IndirectOffsetOnAxis(ap=row_of[:, 0, b:b + 1].bitcast(u32), axis=0),
                                        in_=H[:, b, :], in_offset=None, bounds_check=E - 1, oob_is_err=False
                                        ).then_inc(d_scattered, 16)
            pool.wait_ge(q_stored, 16)
            pool.wait_ge(q_step, 1)
            pool.indirect_dma_start(out=QB[:, 0, 0, :], out_offset=None, in_=Q_dram,
                                    in_offset=bass.IndirectOffsetOnAxis(ap=dst_first[:, :].bitcast(u32), axis=0)).then_inc(q_first, 16)
            pool.wait_ge(p_stored, 16)
            pool.wait_ge(pq_ready, 3)

            def gathers(it, c):
                (slot, used), i = ring(it, c, 4), it * 4 + c
                pool.wait_ge(ld_idx[slot], used * 16 + 16)
                reach(pool, s_step, (i - 3) * G)
                reach(pool, sq_done, i - 3)
                reach(pool, turns, i)
                pool.tensor_tensor(turn, node_id[0:1, 0:1], node_id[0:1, 0:1], ALU.add).then_inc(turns, 1)
                for k in range(G):
                    pool.indirect_dma_start(out=Z[:, slot, k, :], out_offset=None, in_=P_dram,
                                            in_offset=bass.IndirectOffsetOnAxis(ap=src_idx[:, slot, k:k + 1].bitcast(u32), axis=0)
                                            ).then_inc(rows_here[slot], 16)
            chunks(pool, gathers)
            pool.wait_ge(sq_summed, NCH)
            pool.iota(iota_f, pattern=[[1, P]], base=0, channel_multiplier=0,
                      allow_small_or_imprecise_dtypes=True).then_inc(lanes_iota, 1)
            for k in range(2):
                pool.wait_ge(st_s[k], 16 * (NCH // 2 + (k == 0)))
            pool.wait_ge(last_idx, 1)
            for b in range(B):
                pool.indirect_dma_start(out=H[:, b, :], out_offset=None, in_=S_dram,
                                        in_offset=bass.IndirectOffsetOnAxis(ap=row_of[:, 1, b:b + 1].bitcast(u32), axis=0)
                                        ).then_inc(last_here, 16)
            for k, (n0, nn) in enumerate(DST):
                def add_bend(i, c):
                    pool.wait_ge(bend_done, i + (B * k + 1))
                    pool.tensor_tensor(att[:, c % 5, 0:nn], att[:, c % 5, 0:nn], bend[:, c % 2, 0:nn], ALU.add).then_inc(att_added, 1)
                src_blocks(pool, add_bend)

        @block.vector
        def _(dve):
            chain = [0]

            def link(ins):
                chain[0] += 1
                ins.then_inc(dve_chain, 1)
                dve.wait_ge(dve_chain, chain[0])

            def floor_div(out, in_, d):
                link(dve.tensor_scalar(out, in_, 1.0 / d, 0.5 / d - 0.5, ALU.mult, ALU.add))
                link(dve.tensor_scalar(out, out, ROUND, ROUND, ALU.add, ALU.subtract))

            r_w0, r_w1, r_d, r_z, r_cum, r_o, r_next, r_v = (rows[:, k, :] for k in range(8))
            dve.wait_ge(ld_rows, 32)
            floor_div(r_w0, rows_i[:, 0, :], W)
            floor_div(r_w1, rows_i[:, 1, :], W)
            link(dve.tensor_tensor(r_d, r_w1, r_w0, ALU.subtract))
            link(dve.memset(r_z, 0.0))
            link(dve.tensor_tensor_scan(r_cum, r_d, r_z, 0.0, ALU.add, ALU.add))
            dve.wait_ge(pool_consts, 9)
            link(dve.tensor_tensor(r_o, r_cum, r_d, ALU.subtract))
            link(dve.tensor_tensor(r_o, r_o, iota_s[0:1, 0:T], ALU.add))
            link(dve.memset(r_next, 30000.0))
            link(dve.tensor_copy(r_next[:, 0:T - 1], r_o[:, 1:T]))
            dve.tensor_tensor(r_v, r_w0, r_o, ALU.subtract).then_inc(step_rows, 1)
            dve.wait_ge(ld_edges, 48)
            floor_div(f_q, e_src, P)
            link(dve.tensor_scalar(f_r, f_q, -float(P), None, ALU.mult))
            q3 = lambda k: tq[:, k, :, :].rearrange("p c i -> p (c i)")
            link(dve.tensor_tensor(q3(0), f_r, e_src, ALU.add))
            link(dve.tensor_scalar(f_q, f_q, float(W), None, ALU.mult))
            floor_div(f_r, e_dst, W)
            link(dve.tensor_copy(q3(1), f_r))
            link(dve.tensor_scalar(f_r, f_r, -float(W), None, ALU.mult))
            link(dve.tensor_tensor(f_r, f_r, e_dst, ALU.add))
            link(dve.tensor_tensor(q3(2), f_r, f_q, ALU.add))
            dve.wait_ge(step_cols, 1)
            link(dve.tensor_copy(cols, PS[0:RR, 0:3 * RC].rearrange("p (r c) -> p r c", r=3)))
            for c in range(RC):
                link(dve.tensor_scalar(tq[:, 3, c, :], ones[0:RR, :], cols[:, 2, c:c + 1], None, ALU.mult))
                link(dve.tensor_scalar(sel_a, iota_s[0:RR, :], cols[:, 0, c:c + 1], None, ALU.is_ge))
                ins = dve.scalar_tensor_tensor(sel[:, c, :], iota_s[0:RR, :], cols[:, 1, c:c + 1], sel_a, ALU.is_lt, ALU.mult)
                if c == RC - 1:
                    ins.then_inc(tile_tables, 1)
                else:
                    link(ins)
            link(dve.tensor_scalar(below[:, 0, 0:N], iota_n[:, 0:N], run_last, None, ALU.is_ge))
            dve.tensor_scalar(below[:, 1, 0:N], iota_n[:, 0:N], run_last, None, ALU.is_gt).then_inc(runs_below, 1)
            HALF = S // 2
            dve.wait_ge(step_tables, 1)
            for h in range(2):
                s = slice(h * HALF, (h + 1) * HALF)
                ps = [PS[0:P, (4 * h + q) * 512:(4 * h + q) * 512 + HALF] for q in range(4)]
                link(dve.tensor_copy(keyL[:, s], ps[0]))
                link(dve.tensor_tensor(wrow[:, s], ps[3], iota_s[:, s], ALU.add))
                link(dve.tensor_tensor(trow[:, s], ps[1], wrow[:, s], ALU.subtract))
                link(dve.scalar_tensor_tensor(keyR[:, s], trow[:, s], float(B * W), ps[2], ALU.mult, ALU.add))
            link(dve.memset(keyL[:, S:SPAD], -1.0))
            link(dve.memset(keyR[:, S:SPAD], -1.0))
            dve.tensor_scalar(win_addr, wrow[0:1, :], float(NWIN - 1), None, ALU.min).then_inc(step_tables_used, 1)
            dve.wait_ge(step_tables_used, 1)
            dve.wait_ge(runs_below_sum, 1)
            link(dve.tensor_scalar(upto_pos[:, :, :], PS[0:P, 0:2 * B].rearrange("p (q b) -> p q b", q=2), float(P - 1), None, ALU.min))
            link(dve.tensor_scalar(node_edge[:, 0:B], node_id[:, :], 0.5, None, ALU.add))
            link(dve.tensor_scalar(node_edge[:, B:2 * B], node_id[:, :], 0.5, None, ALU.subtract))
            dve.tensor_copy(row_of[:, :, :], upto_pos[:, :, :]).then_inc(run_rows_known, 1)
            dve.memset(CT_words[:, NWORDS - DVE_ZEROS:NWORDS], 0.0).then_inc(counts_zero, 1)

            dve.memset(attr, 1.0).then_inc(attr_ones, 1)
            dve.engine_nop().then_inc(feat_free, 1)
            dve.wait_ge(counts_zero, 4)

            def onehot(slot, n):
                dve.tensor_scalar(onehotR[:, slot, :], iota_w[:, :], keyR[:, bass.ds(n, 1)], None, ALU.is_equal).then_inc(onehots, 1)

            for n in range(AHEAD):
                onehot(n, n)
            dve.engine_nop().then_inc(counts_added, RING)

            def count_adds(first, steps):
                _, win = nc.values_load_multi_w_load_instructions(
                    win_addr[0:1, bass.ds(first, steps)], engines=[mybir.EngineType.DVE], min_val=0, max_val=NWIN - 1,
                    skip_runtime_bounds_check_because="a sorted list's windows, clamped to the last")
                for j in range(steps):
                    if (j + AHEAD) % U == U - 1:
                        dve.tensor_scalar(onehotL[:, U - 1, :], iota_w[:, 0:P], keyL[:, bass.ds(first + (j + AHEAD), 1)], None, ALU.is_equal)
                    onehot((j + AHEAD) % 4, first + (j + AHEAD))
                    dve.wait_ge(step_counts, first + (j + 1))
                    dve.wait_ge(counts_added, first + (j + RING))
                    window = CT[:, :, bass.ds(win[j] * W, W)]
                    dve.tensor_tensor(window, window, PS[0:P, 512 * (j % RING):512 * (j % RING) + B * W].rearrange("p (b w) -> p b w", b=B),
                                      ALU.add).then_inc(counts_added, 1)

            with dve.Fori(0, S // (2 * U)) as it:
                count_adds(it * (2 * U), 2 * U)
            if S % (2 * U):
                count_adds(S - U, U)

            dve.wait_ge(runs_counted, 2 * B)
            link(dve.tensor_scalar(counted, counted, 0.5, 0.5 * T, ALU.mult, ALU.add))
            link(dve.scalar_tensor_tensor(upto_pos[:, :, :], upto_pos[:, :, :], float(T),
                                          counted.rearrange("p (q b) -> p q b", q=2), ALU.mult, ALU.add))

            link(dve.tensor_tensor(deg[:, :], upto_pos[:, 0, :], upto_pos[:, 1, :], ALU.subtract))
            dve.wait_ge(counts_added, S + RING)
            for own in CT_own:
                link(dve.tensor_tensor(own, own, identb[:, :].unsqueeze(1).to_broadcast([P, own.shape[1], P]), ALU.add))
            n_prod, n_chain = [0], [0]

            def over_blocks(v, nb=B):
                return v.unsqueeze(2).to_broadcast([P, nb, D])

            def over_nodes(v, nb=B):
                return v.to_broadcast([P, nb, D])

            def rsqrt(v):
                n_chain[0] += 1
                dve.wait_ge(std_ready, n_chain[0])
                link(dve.reciprocal(v, v))

            def products(use):
                for g in range(NG):
                    dve.wait_ge(prod_psum, n_prod[0] + 1)
                    use(slice(G * g, G * g + G), PO[n_prod[0] % 2][0:P, :, 0:D], g)
                    n_prod[0] += 1
                dve.wait_ge(prod_used, n_prod[0])

            def deviations(bl, nb):
                link(dve.tensor_reduce(lnm[:, bl], X[:, bl, :], AX.X, ALU.add))
                link(dve.tensor_scalar(lnm[:, bl], lnm[:, bl], -1.0 / D, None, ALU.mult))
                link(dve.tensor_tensor(H[:, bl, :], X[:, bl, :], over_blocks(lnm[:, bl], nb), ALU.add))
                link(dve.tensor_tensor(Y[:, bl, :], H[:, bl, :], H[:, bl, :], ALU.mult))
                link(dve.tensor_reduce(lnv[:, bl], Y[:, bl, :], AX.X, ALU.add))

            def layer_norm(known=False, signal=True):
                if not known:
                    deviations(slice(0, B), B)
                dve.tensor_scalar(lnv[:, :], lnv[:, :], 1.0 / D, LN_EPS, ALU.mult, ALU.add).then_inc(var_ready, 1)
                rsqrt(lnv[:, :])
                for g in range(NG):
                    bl = slice(G * g, G * g + G)
                    ins = dve.scalar_tensor_tensor(H[:, bl, :], H[:, bl, :], 0.0, over_blocks(lnv[:, bl], G), ALU.max, ALU.mult)
                    if signal:
                        ins.then_inc(h_ready, 1)
                    else:
                        link(ins)

            def blocks_of(k):
                n0, nn = PB[k]
                return slice(n0 // P, (n0 + nn) // P), nn // P

            def scaled(k):
                bl, nb = blocks_of(k)
                link(dve.tensor_tensor(TMP[k], H[:, bl, :], over_blocks(dinv[:, bl], nb), ALU.mult))
                link(dve.tensor_reduce(maxima[:, k:k + 1], TMP[k].rearrange("p b c -> p (b c)"), AX.X, ALU.max))

            def find_scale():
                link(dve.tensor_reduce(top, maxima, AX.X, ALU.max))
                dve.tensor_scalar(top_spread, ones[:, :], top, None, ALU.mult).then_inc(top_ready, 1)
                dve.wait_ge(prod_psum, n_prod[0] + 1)
                dve.tensor_reduce(top, PO[n_prod[0] % 2][0:P, 0, 0:P], AX.X, ALU.max).then_inc(prod_used, 1)
                n_prod[0] += 1
                dve.wait_ge(prod_used, n_prod[0])
                link(dve.tensor_scalar(top, top, 1.0e-30, None, ALU.max))
                link(dve.tensor_scalar(top.bitcast(i32), top.bitcast(i32), EXPONENT, None, ALU.bitwise_and))
                link(dve.tensor_scalar(unscale, top, 2.0 ** -14, None, ALU.mult))
                link(dve.reciprocal(half_scale, unscale))
                link(dve.tensor_scalar(dinv_unscaled, dinv[:, :], unscale, None, ALU.mult))

            n_split = [0]

            def split(scale, scaled_first):
                reach(dve, agg_psum, len(PB) * n_split[0])
                n_split[0] += 1
                for k in range(len(PB)):
                    bl, nb = blocks_of(k)
                    v = TMP[k] if scaled_first else H[:, bl, :]
                    link(dve.tensor_scalar(SPL[:, 0, bl, :], v, scale, None, ALU.mult))
                    dve.scalar_tensor_tensor(SPL[:, 1, bl, :], v, scale, SPL[:, 0, bl, :], ALU.mult, ALU.subtract
                                             ).then_inc(split_ready, 1)

            def summed_products(use):
                for k in range(len(PB)):
                    bl, nb = blocks_of(k)
                    dve.wait_ge(prod_psum, n_prod[0] + 1)
                    use(k, bl, nb, PO[n_prod[0] % 2][0:P, 0:nb, 0:D])
                    n_prod[0] += 1
                dve.wait_ge(prod_used, n_prod[0])

            s_ = lambda k: ecols[:, k:k + 1]
            dve.wait_ge(stat_sums, NCH)
            dve.wait_ge(ld_e, 48)
            link(dve.tensor_reduce(ecols[:, 3:5], esum, AX.X, ALU.add))
            link(dve.tensor_scalar(ecols[:, 3:5], ecols[:, 3:5], 1.0 / E, None, ALU.mult))
            link(dve.tensor_tensor(s_(5), s_(3), s_(2), ALU.add))
            link(dve.tensor_tensor(s_(5), s_(5), s_(5), ALU.mult))
            link(dve.tensor_tensor(s_(4), s_(4), s_(5), ALU.subtract))
            dve.tensor_scalar(s_(4), s_(4), 0.0, BN_EPS, ALU.max, ALU.add).then_inc(var_ready, 1)
            rsqrt(s_(4))
            link(dve.tensor_tensor(s_(4), s_(4), s_(0), ALU.mult))
            link(dve.tensor_tensor(s_(5), s_(3), s_(4), ALU.mult))
            link(dve.memset(tcol, 0.0))
            dve.tensor_tensor(tcol[:, D:D + 1], s_(1), s_(5), ALU.subtract).then_inc(edge_const, 1)
            dve.wait_ge(edge_const_psum, 1)
            dve.wait_ge(ld_w, 144)
            link(dve.tensor_scalar(W3[:, :], W3[:, :], s_(4), None, ALU.mult))
            link(dve.tensor_tensor(WT[D:D + 1, 7, :], WT[D:D + 1, 7, :], PS[D:D + 1, 0:D], ALU.add))

            dve.tensor_scalar(dinv[:, :], deg[:, :], 1.0, None, ALU.add).then_inc(var_ready, 1)
            rsqrt(dinv[:, :])
            dve.wait_ge(ld_x, 16)
            layer_norm()

            def to_h(bl, ps, g):
                dve.tensor_scalar(H[:, bl, :], ps, 0.0, None, ALU.max).then_inc(prod_used, 1)
            products(to_h)
            dve.wait_ge(ld_p, 16 * 4)
            for k in range(len(PB)):
                scaled(k)
            for l in range(3):
                find_scale()
                split(half_scale, True)
                if l == 1:
                    link(dve.tensor_tensor(X[:, :, :], X[:, :, :], over_nodes(ROWS[:, 3:4, :]), ALU.add))

                def conv(k, bl, nb, ps):
                    dve.tensor_tensor(TMP[k], ps, over_blocks(dinv_unscaled[:, bl], nb), ALU.mult).then_inc(prod_used, 1)
                    dve.wait_ge(prod_used, n_prod[0] + 1)
                    link(dve.tensor_tensor(TMP[k], TMP[k], over_nodes(ROWS[:, l:l + 1, :], nb), ALU.add))
                    ins = dve.scalar_tensor_tensor(H[:, bl, :], TMP[k], 0.0, H[:, bl, :], ALU.max, ALU.add)
                    if k == len(PB) - 1 and l == 2:
                        ins.then_inc(h_ready, 1)
                    else:
                        link(ins)
                    if l < 2:
                        scaled(k)
                summed_products(conv)

            def to_x(bl, ps, g):
                dve.tensor_tensor(X[:, bl, :], ps, X[:, bl, :], ALU.add).then_inc(prod_used, 1)
                dve.wait_ge(prod_used, n_prod[0] + 1)
                deviations(bl, G)
            products(to_x)
            dve.engine_nop().then_inc(layer_done, 1)

            layer_norm(known=True)

            def relu_to_y(bl, ps, g):
                dve.tensor_scalar(Y[:, bl, :], ps, 0.0, None, ALU.max).then_inc(prod_used, 1)
            n_bn = [0]

            def sum_nodes(v, row):
                dve.tensor_reduce(row, v.rearrange("p b c -> p c b"), AX.X, ALU.add).then_inc(y_ready, 1)
                n_bn[0] += 1
                dve.wait_ge(bn_sum, n_bn[0])

            def batch_norm(v, square, gamma, beta, use, then=None):
                mean, scale = bn_rows[:, 0:1, :], bn_rows[:, 1:2, :]
                sum_nodes(v, bn_rows[:, 0, :])
                link(dve.tensor_scalar(mean, PS[0:P, 0:D].unsqueeze(1), 1.0 / N, None, ALU.mult))
                link(dve.tensor_tensor(v, v, over_nodes(mean), ALU.subtract))
                link(dve.tensor_tensor(square, v, v, ALU.mult))
                sum_nodes(square, bn_rows[:, 1, :])
                dve.tensor_scalar(scale, PS[0:P, 0:D].unsqueeze(1), 1.0 / N, BN_EPS, ALU.mult, ALU.add).then_inc(var_ready, 1)
                if then:
                    then()
                rsqrt(scale)
                link(dve.tensor_tensor(scale, scale, gamma, ALU.mult))
                for g in range(NG):
                    bl = slice(G * g, G * g + G)
                    link(dve.tensor_tensor(v[:, bl, :], v[:, bl, :], over_nodes(scale, G), ALU.mult))
                    link(dve.tensor_tensor(v[:, bl, :], v[:, bl, :], over_nodes(beta, G), ALU.add))
                    use(bl)

            def copy_to(t):
                def use(bl, ps, g):
                    dve.tensor_copy(t[:, bl, :], ps).then_inc(prod_used, 1)
                return use
            dve.wait_ge(ld_dst, 16)
            link(dve.tensor_copy(dst_first[:, :], dst_sb[:, 0:1]))
            dve.tensor_tensor(same[:, 1:T], dst_sb[:, 1:T], dst_sb[:, 0:T - 1], ALU.is_equal).then_inc(q_step, 1)
            link(dve.tensor_scalar(lnm[:, :], deg[:, :], 0.5, 1.0e6, ALU.is_lt, ALU.mult))
            link(dve.tensor_tensor(lnm[:, :], lnm[:, :], upto_pos[:, 1, :], ALU.add))
            link(dve.tensor_copy(row_of[:, 0, :], lnm[:, :]))
            link(dve.tensor_scalar(lnm[:, :], upto_pos[:, 0, :], 1.0, 0.0, ALU.subtract, ALU.max))
            dve.tensor_copy(row_of[:, 1, :], lnm[:, :]).then_inc(last_idx, 1)
            dve.wait_ge(last_idx, 1)
            floor_div(lnm[:, :], upto_pos[:, 0, :], T)
            link(dve.tensor_scalar(lnm[:, :], lnm[:, :], -float(T), None, ALU.mult))
            link(dve.tensor_tensor(lnm[:, :], lnm[:, :], upto_pos[:, 0, :], ALU.add))
            link(dve.tensor_scalar(lnm[:, :], lnm[:, :], 0.5, None, ALU.is_gt))
            link(dve.tensor_scalar(valid[:, :], deg[:, :], 0.5, None, ALU.is_gt))
            link(dve.tensor_tensor(valid[:, :], valid[:, :], lnm[:, :], ALU.mult))
            products(copy_to(H))
            dve.engine_nop().then_inc(pq_ready, 1)
            products(copy_to(Y))
            dve.engine_nop().then_inc(pq_ready, 1)
            dve.wait_ge(p_stored, 16)
            products(relu_to_y)
            dve.engine_nop().then_inc(pq_ready, 1)
            dve.wait_ge(ld_p, 16 * 8)
            dve.wait_ge(q_stored, 16)
            dve.wait_ge(d_scattered, 16 * B)
            batch_norm(Y, H, ROWS[:, 0:1, :], ROWS[:, 1:2, :],
                       use=lambda bl: link(dve.tensor_tensor(X[:, bl, :], X[:, bl, :], Y[:, bl, :], ALU.add)),
                       then=lambda: dve.memset(ea, 1.0).then_inc(ea_ones, 1))
            dve.engine_nop().then_inc(node_part_done, 1)

            def step_q(it, c, k):
                slot, i = c % 2, it * 4 + c
                if isinstance(i, int) and i + k == 0:
                    dve.wait_ge(q_first, 16)
                    return
                prev = QB[:, slot, k - 1, :] if k else QB[:, 1 - slot, G - 1, :]
                dve.wait_ge(q_step, i * G + k)
                dve.scalar_tensor_tensor(QB[:, slot, k, :], prev, same[:, bass.ds(i * G + k, 1)], Dr[:, slot, k, :],
                                         ALU.mult, ALU.add).then_inc(q_step, 1)

            def step_s(it, c, k):
                (slot, used), i, y = ring(it, c, 2), it * 4 + c, Z[:, c % 4, k, :]
                if k == 0:
                    dve.wait_ge(y_done, i + 1)
                    reach(dve, st_s[slot], used * 16)
                if isinstance(i, int) and i + k == 0:
                    dve.tensor_copy(SO[:, 0, 0, :], y).then_inc(s_step, 1)
                    return
                prev = SO[:, slot, k - 1, :] if k else SO[:, 1 - slot, G - 1, :]
                dve.wait_ge(s_step, i * G + k)
                dve.scalar_tensor_tensor(SO[:, slot, k, :], prev, same[:, bass.ds(i * G + k, 1)], y,
                                         ALU.mult, ALU.add).then_inc(s_step, 1)

            def add_squares(it, c):
                i = it * 4 + c
                dve.wait_ge(sq_done, i + 1)
                if isinstance(i, int) and i == 0:
                    dve.tensor_copy(sq_acc, Y2).then_inc(sq_summed, 1)
                    return
                dve.wait_ge(sq_summed, i)
                dve.tensor_tensor(sq_acc, sq_acc, Y2, ALU.add).then_inc(sq_summed, 1)

            def edge_step(it, c):
                (slot, used), i, z = ring(it, c, 4), it * 4 + c, Z[:, c % 4, :, :]
                dve.wait_ge(rpart_psum, i + 1)
                dve.wait_ge(rows_here[slot], used * (16 * G) + 16 * G)
                dve.tensor_tensor(z, psR[c % 2], z, ALU.add).then_inc(src_in, 1)
                dve.wait_ge(ld_d[c % 2], ring(it, c, 2)[1] * 16 + 16)
                for k in range(G):
                    step_q(it, c, k)
                    if c:
                        step_s(it, c - 1, k)
                dve.wait_ge(q_step, i * G + G)
                dve.wait_ge(src_in, i + 1)
                dve.tensor_tensor(z, z, QB[:, c % 2, :, :], ALU.add).then_inc(z_ready, 1)
                if c:
                    add_squares(it, c - 1)
            chunks(dve, edge_step)
            for k in range(G):
                step_s((NCH - 9) // 4, 8, k)
            add_squares((NCH - 9) // 4, 8)

            mean, scale = bn_rows[:, 0, :], bn_rows[:, 1, :]
            dve.wait_ge(s_step, T)
            dve.wait_ge(sq_total, 1)
            dve.tensor_reduce(scale, msg_sq.rearrange("p (k c) -> p c k", k=G), AX.X, ALU.add).then_inc(sq_read, 1)

            dve.wait_ge(lanes_iota, 1)
            dve.wait_ge(ld_last, 16)
            link(dve.tensor_copy(lnm[:, 0:1], dst_last))
            link(dve.tensor_scalar(lnv[:, :], node_id[:, :], node_id[:, 0:1], None, ALU.subtract))
            link(dve.tensor_scalar(lnv[:, :], lnv[:, :], lnm[:, 0:1], -1.0, ALU.subtract, ALU.mult))
            dve.wait_ge(st_s[1], 16 * (NCH // 2))
            for b in range(B):
                dve.tensor_scalar(tail_hot[b], iota_f, lnv[:, b:b + 1], None, ALU.is_equal).then_inc(tails_hot, 1)

            def tails(bl, ps, g):
                dve.tensor_copy(TAILS[:, bl, :], ps).then_inc(prod_used, 1)
            products(tails)
            dve.wait_ge(last_here, 16 * B)
            link(dve.tensor_tensor(H, H, over_blocks(valid[:, :]), ALU.mult))
            link(dve.tensor_tensor(H, H, TAILS, ALU.add))

            sum_nodes(H, mean)
            dve.wait_ge(sq_read, 1)
            link(dve.tensor_copy(mean, PS[0:P, 0:D]))
            link(dve.tensor_scalar(bn_rows[:, :, :], bn_rows[:, :, :], 1.0 / E, None, ALU.mult))
            link(dve.tensor_tensor(msq, mean, mean, ALU.mult))
            link(dve.tensor_tensor(scale, scale, msq, ALU.subtract))
            dve.tensor_scalar(scale, scale, 0.0, BN_EPS, ALU.max, ALU.add).then_inc(var_ready, 1)
            rsqrt(scale)
            link(dve.tensor_tensor(scale, scale, ROWS[:, 2, :], ALU.mult))
            link(dve.tensor_tensor(msq, mean, scale, ALU.mult))
            link(dve.tensor_tensor(mean, ROWS[:, 3, :], msq, ALU.subtract))
            link(dve.tensor_tensor(H, H, over_nodes(bn_rows[:, 1:2, :]), ALU.mult))
            link(dve.tensor_tensor(X[:, :, :], X[:, :, :], H, ALU.add))
            link(dve.tensor_tensor(H, over_blocks(deg[:, :]), over_nodes(bn_rows[:, 0:1, :]), ALU.mult))
            link(dve.tensor_tensor(X[:, :, :], X[:, :, :], H, ALU.add))
            dve.engine_nop().then_inc(layer_done, 1)

            layer_norm()

            dve.wait_ge(ld_p, 16 * 12)
            dve.wait_ge(ld_w, 208)
            for k in range(2):
                link(dve.tensor_tensor(W3[:, :], WT[0:D, 0, :], ROWS[0:D, k, :], ALU.mult))
                link(dve.tensor_reduce(ecols[:, k:k + 1], W3[:, :], AX.X, ALU.add))
            dve.engine_nop().then_inc(att_w, 1)

            def to_hs(bl, ps, g):
                logit_parts = PO[n_prod[0] % 2][0:P, :, D:D + 2]
                for k, col in enumerate((a_src, a_dst)):
                    dve.tensor_copy(col[:, bl], logit_parts[:, :, k:k + 1].rearrange("p b o -> p (b o)"))
                dve.tensor_copy(HS[:, bl, 0:D], ps).then_inc(prod_used, 1)
            products(to_hs)
            link(dve.memset(HS[:, :, D:D + 1], 1.0))
            link(dve.tensor_reduce(ends[:, 0:1], a_src, AX.X, ALU.max))
            link(dve.tensor_reduce(ends[:, 1:2], a_src, AX.X, ALU.min))
            link(dve.tensor_scalar(ends[:, 1:2], ends[:, 1:2], -1.0, None, ALU.mult))
            for r in range(2):
                dve.tensor_scalar(diag[:, 0, r, :], ident[:, :], ends[:, r:r + 1], None, ALU.mult).then_inc(ends_ready, 1)
            link(dve.tensor_scalar(a_src_bend, a_src, NEG_SLOPE - 1.0, None, ALU.mult))
            dve.wait_ge(ends_psum, 1)
            link(dve.tensor_reduce(ends, att_rows[0][0][:, 0:2 * P].rearrange("p (r n) -> p r n", r=2), AX.X, ALU.max))
            link(dve.tensor_tensor(span, ends[:, 0:1], ends[:, 1:2], ALU.add))
            link(dve.tensor_scalar(span, span, 4.0, 1.0e-30, ALU.mult, ALU.max))
            link(dve.reciprocal(inv_span, span))
            link(dve.tensor_scalar(a_src_key, a_src, ends[:, 1:2], inv_span, ALU.add, ALU.mult))
            dve.tensor_scalar(a_src_key, a_src_key, 0.5, None, ALU.add).then_inc(att_cols, 1)
            dve.wait_ge(att_cols, 1)

            def greatest(k, i, c):
                (n0, nn), side = DST[k], acc[:, k % 2, 0:DST[k][1]].unsqueeze(1)
                counts, key = CT[:, bass.ds(i, 1), n0:n0 + nn], a_src_key[:, bass.ds(i, 1)]
                if isinstance(i, int) and i == 0:
                    reach(dve, acc_T, k - 1)
                    dve.tensor_scalar(side, counts, key, None, ALU.min).then_inc(max_step, 1)
                else:
                    dve.wait_ge(max_step, i + B * k)
                    dve.scalar_tensor_tensor(side, counts, key, side, ALU.min, ALU.max).then_inc(max_step, 1)

            def dst_terms(k):
                n0, nn = DST[k]
                nc_, bl = nn // P, slice(n0 // P, (n0 + nn) // P)
                top = cmax[:, 0:nc_]

                def diagonals(r, col):
                    for c in range(nc_):
                        dve.tensor_scalar(diag[:, r, c, :], ident[:, :], col[:, c:c + 1], None, ALU.mult).then_inc(diag_ready, 1)

                link(dve.tensor_scalar(dst_bend[:, 0:nc_], a_dst[:, bl], NEG_SLOPE - 1.0, None, ALU.mult))
                reach(dve, row_psum, 2 * k)
                diagonals(1, dst_bend)
                dve.wait_ge(acc_T, k + 1)
                link(dve.tensor_reduce(top, PSA[:, 0:nc_, 0:P], AX.X, ALU.max))
                link(dve.tensor_scalar(top, top, 0.5, span, ALU.subtract, ALU.mult))
                link(dve.scalar_tensor_tensor(top, top, ends[:, 1:2], a_dst[:, bl], ALU.subtract, ALU.add))
                link(dve.scalar_tensor_tensor(top, top, NEG_SLOPE, top, ALU.mult, ALU.max))
                link(dve.tensor_tensor(cm[:, 0:nc_], a_dst[:, bl], top, ALU.subtract))
                diagonals(0, cm)

            def step_of(k):
                n0, nn = DST[k]

                def bounded(i, c):
                    v = att[:, c % 5, 0:nn]
                    dve.wait_ge(att_added, i + (B * k + 1))
                    dve.tensor_scalar(v, v, LOGIT_BOUND, None, ALU.min).then_inc(att_bounded, 1)

                def weights(i, c):
                    w = att[:, c % 5, 0:nn].unsqueeze(1)
                    dve.wait_ge(exp_done, i + (B * k + 1))
                    dve.tensor_tensor(w, w, CT[:, bass.ds(i, 1), n0:n0 + nn], ALU.mult).then_inc(w_done, 1)

                def step(i, c):
                    if k + 1 < len(DST):
                        greatest(k + 1, i, c)
                    if not isinstance(i, int) or i >= 3:
                        weights(i - 3, c - 3)
                    if not isinstance(i, int) or i >= 1:
                        bounded(i - 1, c - 1)
                return step, weights, bounded

            def add_attention(k):
                n0, nn = DST[k]
                bl = slice(n0 // P, (n0 + nn) // P)
                dve.wait_ge(tanh_done, k + 1)
                link(dve.tensor_tensor(X[:, bl, :], X[:, bl, :], OX[:, 0:nn // P, :], ALU.add))

            src_blocks(dve, lambda i, c: greatest(0, i, c))
            dst_terms(0)
            for k, (n0, nn) in enumerate(DST):
                nc_, bl = nn // P, slice(n0 // P, (n0 + nn) // P)
                step, weights, bounded = step_of(k)
                src_blocks(dve, step)
                weights(B - 3, B - 3)
                bounded(B - 1, B - 1)
                if k + 1 < len(DST):
                    dst_terms(k + 1)
                for i in range(B - 2, B):
                    weights(i, i)
                if k:
                    add_attention(k - 1)
                dve.wait_ge(att_psum, B * (k + 1))
                sums = PSO[k % 2]
                link(dve.tensor_scalar(lnm[:, 0:nc_], sums[:, 0:nc_, D:D + 1].rearrange("p k o -> p (k o)"), SOFTMAX_EPS, None, ALU.add))
                link(dve.reciprocal(lnm[:, 0:nc_], lnm[:, 0:nc_]))
                link(dve.tensor_tensor(OX[:, 0:nc_, :], sums[:, 0:nc_, 0:D], over_blocks(lnm[:, 0:nc_], nc_), ALU.mult))
                dve.tensor_tensor(OX[:, 0:nc_, :], OX[:, 0:nc_, :], over_nodes(ROWS[:, 2:3, :], nc_), ALU.add).then_inc(ox_ready, 1)
            add_attention(len(DST) - 1)
            for own in CT_own:
                link(dve.tensor_tensor(own, own, identb[:, :].unsqueeze(1).to_broadcast([P, own.shape[1], P]), ALU.subtract))
            dve.engine_nop().then_inc(layer_done, 1)

            layer_norm(signal=False)
            split(LN_SCALE, False)
            dve.engine_nop().then_inc(h_ready, 1)
            link(dve.tensor_scalar(lnm[:, :], deg[:, :], 1.0, LN_SCALE, ALU.max, ALU.mult))
            link(dve.reciprocal(lnm[:, :], lnm[:, :]))

            def own_part(bl, ps, g):
                dve.tensor_tensor(H[:, bl, :], ps, over_nodes(ROWS[:, 3:4, :], G), ALU.add).then_inc(prod_used, 1)
            products(own_part)

            def mean_part(k, bl, nb, ps):
                dve.tensor_tensor(TMP[k], ps, over_blocks(lnm[:, bl], nb), ALU.mult).then_inc(prod_used, 1)
                dve.wait_ge(prod_used, n_prod[0] + 1)
                link(dve.tensor_tensor(H[:, bl, :], TMP[k], H[:, bl, :], ALU.add))
            summed_products(mean_part)
            dve.wait_ge(ld_p, 16 * 14)
            batch_norm(H, Y, ROWS[:, 0:1, :], ROWS[:, 1:2, :],
                       use=lambda bl: dve.scalar_tensor_tensor(X[:, bl, :], H[:, bl, :], 0.0, X[:, bl, :], ALU.max, ALU.add
                                                               ).then_inc(out_ready, 1))

        @block.tensor
        def _(pe):
            pe.wait_ge(step_rows, 1)
            pe.wait_ge(pool_consts, 9)
            for k, r in enumerate((5, 6, 7)):
                for c in range(RC):
                    last = pe.matmul(PS[0:RR, k * RC + c:k * RC + c + 1], rows[:, r, c * RR:(c + 1) * RR], ones[0:1, 0:1],
                                     start=True, stop=True)
            last.then_inc(step_cols, 1)
            pe.wait_ge(tile_tables, 1)
            HALF = S // 2
            for h in range(2):
                for q in range(4):
                    for c in range(RC):
                        last = pe.matmul(PS[0:P, (4 * h + q) * 512:(4 * h + q) * 512 + HALF], tq[:, q, c, :],
                                         sel[:, c, h * HALF:(h + 1) * HALF], start=(c == 0), stop=(c == RC - 1))
            last.then_inc(step_tables, 1)
            pe.wait_ge(runs_below, 1)
            pe.wait_ge(step_tables_used, 1)
            for q in range(2):
                for b in range(B):
                    last = pe.matmul(PS[0:P, q * B + b:q * B + b + 1], below[:, q, b * P:(b + 1) * P], ones_b, start=True, stop=True)
            last.then_inc(runs_below_sum, 1)
            pe.wait_ge(run_rows_known, 1)

            def count_step(it, j):
                pe.wait_ge(onehots, it * U + (j + 1))
                if j % 4 == 0:
                    pe.wait_ge(left_hot, it * 2 + (j // 4 + 1))
                pe.wait_ge(counts_added, it * U + (j + 1))
                pe.matmul(PS[0:P, 512 * (j % RING):512 * (j % RING) + B * W], onehotL[:, j, :], onehotR[:, j % 4, :],
                          start=True, stop=True).then_inc(step_counts, 1)

            stats = NCH
            pe.wait_ge(ld_e, 48)
            with pe.Fori(0, stats) as it:
                for j in range(U):
                    count_step(it, j)
                    if j == 0:
                        pe.wait_ge(ld_attr, it * 16 + 16)
                        pe.wait_ge(feat_free, it + 1)
                    if j < G:
                        last = pe.matmul(psF[:, j, :], eW[:, :], attr[:, j * P:(j + 1) * P], start=True, stop=True)
                    if j == G - 1:
                        last.then_inc(stat_pre, 1)
            with pe.Fori(stats, S // U) as it:
                for j in range(U):
                    count_step(it, j)

            n_t, n_prod, n_agg = [0], [0], [0]
            n_h = [0]

            def transposes(grouped=False):
                pe.wait_ge(prod_used, n_prod[0]) if n_prod[0] else None
                for g in range(NG):
                    if g == 0 or grouped:
                        n_h[0] += 1
                        pe.wait_ge(h_ready, n_h[0])
                    if n_t[0] >= 2:
                        pe.wait_ge(hT_sbuf, n_t[0] - 1)
                    for k in range(G):
                        last = pe.transpose(PT[n_t[0] % 2][0:D, k, 0:P], H[:, g * G + k, :], ident[:, :])
                    last.then_inc(hT_psum, 1)
                    n_t[0] += 1
                pe.wait_ge(hT_sbuf, n_t[0])

            def products(w, rows_in, more=None):
                for g in range(NG):
                    if n_prod[0] >= 2:
                        pe.wait_ge(prod_used, n_prod[0] - 1)
                    for k in range(G):
                        n0 = (g * G + k) * P
                        last = pe.matmul(PO[n_prod[0] % 2][0:P, k, 0:D], TB[0:rows_in, n0:n0 + P], WT[0:rows_in, w, :],
                                         start=True, stop=True)
                        if more is not None:
                            last = pe.matmul(PO[n_prod[0] % 2][0:P, k, D:D + 2], TB[0:D, n0:n0 + P], more, start=True, stop=True)
                    last.then_inc(prod_psum, 1)
                    n_prod[0] += 1

            def edge_sums(w):
                done = len(PB) * n_agg[0]
                n_agg[0] += 1

                def src_block(k, b, first=False, final=False):
                    n0, nn = PB[k]
                    for s in range(2):
                        last = pe.matmul(PS[0:D, 512 * (k % 4):512 * (k % 4) + nn],
                                         SPL[:, s, b, :] if isinstance(b, int) else SPL[:, s, bass.ds(b, 1), :].rearrange("p o c -> p (o c)"),
                                         CT[:, b, n0:n0 + nn] if isinstance(b, int) else CT[:, bass.ds(b, 1), n0:n0 + nn].rearrange("p o n -> p (o n)"),
                                         start=first and s == 0, stop=final and s == 1)
                    return last

                def product(k):
                    n0, nn = PB[k]
                    pe.wait_ge(agg_sbuf, done + k + 1)
                    reach(pe, prod_used, n_prod[0] - 1)
                    for c in range(nn // P):
                        last = pe.matmul(PO[n_prod[0] % 2][0:P, c, 0:D], TB[0:D, n0 + c * P:n0 + (c + 1) * P], WT[0:D, w, :],
                                         start=True, stop=True)
                    last.then_inc(prod_psum, 1)
                    n_prod[0] += 1

                for k in range(len(PB)):
                    reach(pe, agg_sbuf, done + k - 3)
                    if k == 0:
                        for b in range(B - 1):
                            if b % 4 == 0:
                                pe.wait_ge(split_ready, done + b // 4 + 1)
                            src_block(k, b, first=b == 0)
                        pe.wait_ge(split_ready, done + len(PB))
                    else:
                        for b in range(4):
                            src_block(k, b, first=b == 0)
                        product(k - 1)
                        with pe.Fori(0, 4) as it:
                            for j in range(5):
                                src_block(k, it * 5 + (j + 4))
                    src_block(k, B - 1, final=True).then_inc(agg_psum, 1)
                product(len(PB) - 1)

            pe.wait_ge(ld_w, 144)
            pe.wait_ge(counts_added, RING + S)
            pe.wait_ge(edge_const, 1)
            pe.matmul(PS[0:D + 1, 0:D], tcol, W3[:, :], start=True, stop=True).then_inc(edge_const_psum, 1)
            pe.wait_ge(tb_ones, 1)
            transposes(grouped=True)
            products(0, D + 1)
            for l in range(3):
                pe.wait_ge(top_ready, l + 1)
                reach(pe, prod_used, n_prod[0] - 1)
                pe.matmul(PO[n_prod[0] % 2][0:P, 0, 0:P], top_spread, ident[:, :], start=True, stop=True).then_inc(prod_psum, 1)
                n_prod[0] += 1
                edge_sums(1 + l)
            transposes()
            products(4, D)
            transposes(grouped=True)
            pe.wait_ge(tb_ones, 2)
            products(7, D + 1)
            products(6, D)
            products(5, D + 1)
            n_bn = [0]

            def sums_over_lanes(*rows):
                for r in rows:
                    n_bn[0] += 1
                    pe.wait_ge(y_ready, n_bn[0])
                    pe.matmul(PS[0:P, 0:D], ones[:, :], bn_rows[:, r, :], start=True, stop=True).then_inc(bn_sum, 1)
            sums_over_lanes(0, 1)
            pe.wait_ge(prod_used, n_prod[0])

            def pre(it, c):
                (slot, used), i = ring(it, c, 2), it * 4 + c
                pe.wait_ge(ld_ea[slot], used * 16 + 16)
                reach(pe, pre_relu, i)
                for k in range(G):
                    last = pe.matmul(psE[:, k, :], eW[:, :], ea[:, slot, k * P:(k + 1) * P], start=True, stop=True)
                last.then_inc(pre_psum, 1)

            def edge_step(it, c):
                i = it * 4 + c
                pe.wait_ge(pre_relu, i + 1)
                reach(pe, src_in, i - 1)
                for k in range(G):
                    last = pe.matmul(psR[c % 2][:, k, :], RE[:, c % 2, k * P:(k + 1) * P], W3[:, :], start=True, stop=True)
                last.then_inc(rpart_psum, 1)
                if before(it, c + 1):
                    pre(it, c + 1)
            pre(0, 0)
            chunks(pe, edge_step)
            pe.wait_ge(sq_summed, NCH)
            pe.matmul(msg_sq, ones[:, :], sq_acc, start=True, stop=True).then_inc(sq_total, 1)
            pe.wait_ge(s_step, T)
            pe.wait_ge(sq_read, 1)
            for g in range(NG):
                pe.wait_ge(tails_hot, G * (g + 1))
                if g >= 2:
                    pe.wait_ge(prod_used, n_prod[0] - 1)
                for k in range(G):
                    last = pe.matmul(PO[n_prod[0] % 2][0:P, k, 0:D], tail_hot[g * G + k], SO[:, 0, G - 1, :], start=True, stop=True)
                last.then_inc(prod_psum, 1)
                n_prod[0] += 1
            sums_over_lanes(0)
            transposes(grouped=True)
            pe.wait_ge(ld_w, 208)
            pe.wait_ge(att_w, 1)
            products(0, D, more=ecols[:, 0:2])
            pe.wait_ge(prod_used, n_prod[0])
            def transposed_max(k):
                pe.wait_ge(max_step, B * (k + 1))
                for c in range(DST[k][1] // P):
                    last = pe.transpose(PSA[:, c, 0:P], acc[:, k % 2, c * P:(c + 1) * P], ident[:, :])
                last.then_inc(acc_T, 1)

            def dst_rows(k):
                nn, before_k = DST[k][1], sum(n for _, n in DST[:k]) // P
                for n, r in enumerate((1, 0)):
                    pe.wait_ge(diag_ready, 2 * before_k + (n + 1) * nn // P)
                    pe.matmul(att_rows[k % 2][r][:, 0:nn], ones[:, :], diag[:, r, 0:nn // P, :].rearrange("p c n -> p (c n)"),
                              start=True, stop=True).then_inc(row_psum, 1)

            pe.wait_ge(ends_ready, 2)
            pe.matmul(att_rows[0][0][:, 0:2 * P], ones[:, :], diag[:, 0, 0:2, :].rearrange("p c n -> p (c n)"),
                      start=True, stop=True).then_inc(ends_psum, 1)
            transposed_max(0)
            dst_rows(0)
            for k, (n0, nn) in enumerate(DST):
                nc_ = nn // P
                reach(pe, ox_ready, k - 1)

                def weighted(i, slot):
                    if isinstance(i, int) and k + 1 < len(DST):
                        if i == B - 3:
                            transposed_max(k + 1)
                        if i == B - 2:
                            dst_rows(k + 1)
                    pe.wait_ge(w_done, i + (B * k + 1))
                    for c in range(nc_):
                        last = pe.matmul(PSO[k % 2][:, c, 0:D + 1], att[:, slot % 5, c * P:(c + 1) * P],
                                         HS[:, bass.ds(i, 1), :].rearrange("p o c -> p (o c)"),
                                         start=isinstance(i, int) and i + c == 0, stop=False)
                    last.then_inc(att_psum, 1)

                src_blocks(pe, weighted, last=False)
                pe.wait_ge(w_done, B * (k + 1))
                for c in range(nc_):
                    last = pe.matmul(PSO[k % 2][:, c, 0:D + 1], att[:, (B - 1) % 5, c * P:(c + 1) * P], HS[:, B - 1, :],
                                     start=False, stop=c == nc_ - 1)
                last.then_inc(att_psum, 1)
            transposes()
            products(1, D)
            edge_sums(2)
            sums_over_lanes(0, 1)

        @block.scalar
        def _(act):
            n_t, n_prod, n_agg, n_var = [0], [0], [0], [0]

            def root(v):
                n_var[0] += 1
                act.wait_ge(var_ready, n_var[0])
                act.activation(v, v, ACT.Sqrt).then_inc(std_ready, 1)

            def transposes():
                if n_prod[0]:
                    act.wait_ge(prod_psum, n_prod[0])
                for g in range(NG):
                    act.wait_ge(hT_psum, n_t[0] + 1)
                    act.activation(TB[0:D, g * G * P:(g + 1) * G * P].rearrange("p (k n) -> p k n", k=G),
                                   PT[n_t[0] % 2][0:D, :, 0:P], ACT.Copy).then_inc(hT_sbuf, 1)
                    n_t[0] += 1

            def ones_row():
                act.activation(TB[D:D + 1, :], ones[D:D + 1, 0:1].to_broadcast([1, N]), ACT.Copy).then_inc(tb_ones, 1)

            def agg_out():
                for k, (n0, nn) in enumerate(PB):
                    act.wait_ge(agg_psum, n_agg[0] + 1)
                    act.activation(TB[0:D, n0:n0 + nn], PS[0:D, 512 * (k % 4):512 * (k % 4) + nn], ACT.Copy).then_inc(agg_sbuf, 1)
                    n_agg[0] += 1

            def left_onehots(it, h):
                reach(act, left_hot, it * 2 + (h - 1))
                js = range(4 * h, 4 * h + 4 - h)
                for j in js:
                    act.activation(dist[:, j, :], iota_w[:, 0:P], ACT.Abs, bias=keyL[:, bass.ds(it * U + j, 1)],
                                   scale=-1.0).then_inc(left_dist, 1)
                act.wait_ge(left_dist, it * (U - 1) + js[-1] + 1)
                reach(act, step_counts, it * U + 4 * (h - 1))
                act.activation(onehotL[:, js[0]:js[-1] + 1, :], dist[:, js[0]:js[-1] + 1, :], ACT.Relu,
                               bias=ones[:, 0:1], scale=-1.0).then_inc(left_hot, 1)

            def count_row(it, r):
                act.wait_ge(run_rows_here[r], it * 16 + 16)
                act.activation(run_ring[:, r, :], run_ring[:, r, :], ACT.Sign, bias=node_edge[:, bass.ds(it * 2 + r, 1)],
                               scale=-1.0, accum_out=counted[:, bass.ds(it * 2 + r, 1)]).then_inc(runs_counted, 1)

            act.wait_ge(run_rows_known, 1)
            act.activation(CT_words[:, NWORDS - SETUP + POOL_ZEROS:NWORDS - DVE_ZEROS],
                           ones[0:P, 0:1].to_broadcast([P, SETUP - POOL_ZEROS - DVE_ZEROS]), ACT.Copy, scale=0.0).then_inc(counts_zero, 1)
            act.wait_ge(runs_below_sum, 1)

            def feature_sum(i):
                act.wait_ge(stat_pre, i + 1)
                reach(act, stat_sums, i)
                act.activation(feat.rearrange("p (k n) -> p k n", k=G), psF, ACT.Relu,
                               accum_out=esum[:, 0, bass.ds(i, 1)]).then_inc(feat_free, 1)

            def feature_squares(i):
                act.wait_ge(feat_free, i + 2)
                if isinstance(i, int):
                    act.activation(ecols[:, 2:3], esum[:, 0, 0:1], ACT.Copy, scale=-1.0 / (G * P)).then_inc(edge_shift, 1)
                    act.wait_ge(edge_shift, 1)
                act.activation(feat_sq, feat, ACT.Square, bias=ecols[:, 2:3],
                               accum_out=esum[:, 1, bass.ds(i, 1)]).then_inc(stat_sums, 1)

            def round_of(it, rows, stats=True):
                left_onehots(it + 1, 0)
                if rows:
                    count_row(it, 0)
                if stats:
                    feature_sum(it)
                left_onehots(it + 1, 1)
                if rows:
                    count_row(it, 1)
                if stats:
                    feature_squares(it)
            left_onehots(0, 0)
            left_onehots(0, 1)
            round_of(0, True)
            with act.Fori(1, B) as it:
                round_of(it, True)
            with act.Fori(B, NCH) as it:
                round_of(it, False)
            with act.Fori(NCH, S // U - 1) as it:
                round_of(it, False, False)
            root(ecols[:, 4:5])
            act.wait_ge(d_zero, 16 * NCH)
            root(dinv[:, :])
            root(lnv[:, :])
            ones_row()
            transposes()
            n_prod[0] += NG
            for l in range(3):
                agg_out()
                n_prod[0] += len(PB) + 1
            transposes()
            ones_row()
            n_prod[0] += NG
            root(lnv[:, :])
            transposes()
            n_prod[0] += 3 * NG
            root(bn_rows[:, 1:2, :])

            def features(it, c):
                i = it * 4 + c
                act.wait_ge(pre_psum, i + 1)
                reach(act, rpart_psum, i - 1)
                if isinstance(i, int) and i == 1:
                    act.wait_ge(node_part_done, 1)
                act.activation(RE[:, c % 2, :].rearrange("p (k n) -> p k n", k=G), psE, ACT.Relu).then_inc(pre_relu, 1)

            def edge_step(it, c):
                i, y = it * 4 + c, Z[:, c % 4, :, :].rearrange("p k c -> p (k c)")
                if before(it, c + 1):
                    features(it, c + 1)
                act.wait_ge(z_ready, i + 1)
                act.activation(y, y, ACT.Relu).then_inc(y_done, 1)
                act.wait_ge(y_done, i + 1)
                reach(act, sq_summed, i)
                act.activation(Y2, y, ACT.Square).then_inc(sq_done, 1)
            features(0, 0)
            chunks(act, edge_step)
            root(bn_rows[:, 1, :])
            n_prod[0] += NG
            root(lnv[:, :])
            transposes()
            n_prod[0] += NG

            def step_of(k):
                nn = DST[k][1]

                def exponent(i, c):
                    act.wait_ge(att_bounded, i + (B * k + 1))
                    act.activation(att[:, c % 5, 0:nn], att[:, c % 5, 0:nn], ACT.Exp).then_inc(exp_done, 1)

                def step(i, c):
                    if isinstance(i, int) and i == 0:
                        act.wait_ge(row_psum, 2 * k + 2)
                    reach(act, att_psum, i + (B * k - 4))
                    act.activation(att[:, c % 5, 0:nn], att_rows[k % 2][0][:, 0:nn], ACT.Identity, bias=a_src[:, bass.ds(i, 1)])
                    reach(act, att_added, i + (B * k - 1))
                    act.activation(bend[:, c % 2, 0:nn], att_rows[k % 2][1][:, 0:nn], ACT.Relu,
                                   bias=a_src_bend[:, bass.ds(i, 1)]).then_inc(bend_done, 1)
                    if not isinstance(i, int) or i >= 2:
                        exponent(i - 2, c - 2)
                return step, exponent

            def tanh_of(k):
                act.wait_ge(ox_ready, k + 1)
                ox = OX[:, 0:DST[k][1] // P, :]
                act.activation(ox, ox, ACT.Tanh).then_inc(tanh_done, 1)

            act.wait_ge(att_cols, 1)
            for k, (n0, nn) in enumerate(DST):
                nc_ = nn // P
                step, exponent = step_of(k)
                src_blocks(act, step)
                for i in range(B - 2, B):
                    exponent(i, i)
                if k:
                    tanh_of(k - 1)
            tanh_of(len(DST) - 1)
            root(lnv[:, :])
            transposes()
            n_prod[0] += NG
            agg_out()
            n_prod[0] += len(PB)
            root(bn_rows[:, 1:2, :])


def layout(i):
    def c(a):
        return np.ascontiguousarray(a)
    zeros = np.zeros(D, np.float32)
    gcn = "L0_gnn_gcn_"
    weights = [i["L0_gnn_W_in"].T, *(i[gcn + "W"][k].T for k in range(3)), i["L0_gnn_W_out"].T, i["L1_gnn_W_node"],
               i["L1_gnn_W_msg"][0:D], i["L1_gnn_W_msg"][D:2 * D], i["L2_gnn_W"], i["L3_gnn_Wr"].T, i["L3_gnn_Wl"].T]
    rows = [i["L0_gnn_b_in"], zeros, zeros, zeros, i["L0_gnn_b_out"], i["L1_gnn_b_node"], zeros, i["L1_gnn_b_msg"],
            zeros, i["L3_gnn_bl"], zeros, *i[gcn + "b"],
            *(i["L1_gnn_" + k] for k in ("g_node", "beta_node", "g_msg", "beta_msg")),
            *(i["L2_gnn_" + k] for k in ("att_src", "att_dst", "bias")), i["L3_gnn_gamma"], i["L3_gnn_beta"]]
    return dict(x=c(i["x"]), dst_tiles=c(i["dst"].reshape(T, P)), src_tiles=c(i["src"].reshape(T, P)),
                dst_lanes=c(i["dst"].reshape(T, P).T), dst_runs=c(i["dst"].reshape(P, T)),
                src_runs=c(i["src"].reshape(P, T)),
                edge_attr_T=c(i["edge_attr_4"].reshape(P, T, DE).transpose(2, 1, 0).reshape(DE, E)),
                weights_T=c(np.stack(weights)), weights_msg_edge=c(i["L1_gnn_W_msg"][2 * D:]),
                edge_W=c(np.concatenate([i["L1_gnn_W_edge"], i["L1_gnn_b_edge"][None]])),
                edge_cols=c(np.stack([i["L1_gnn_g_edge"], i["L1_gnn_beta_edge"]], 1)), bias_rows=c(np.stack(rows)))


def kernel(**inputs):
    import concourse.bacc as bacc
    from concourse.bass_utils import run_bass_kernel_spmd

    arrays = layout({name: np.asarray(a) for name, a in inputs.items()})
    nc = bacc.Bacc("TRN2", target_bir_lowering=False, num_devices=1)
    tensors = {name: nc.dram_tensor(name, a.shape, mybir.dt.from_np(a.dtype), kind="ExternalInput").ap()
               for name, a in arrays.items()}
    out = nc.dram_tensor("out", (N, D), mybir.dt.float32, kind="ExternalOutput").ap()
    build_program(nc, **tensors, out=out)
    return run_bass_kernel_spmd(nc, [arrays], core_ids=[0]).results[0]["out"]
```
